# Optimizing a Trainium2 kernel written in Bass

```python
import numpy as np
import jax
import jax.numpy as jnp

def _softmax(x, axis=-1):
    return jax.nn.softmax(x, axis=axis)

def _gelu(x):
    return jax.nn.gelu(x, approximate=True)

def _silu(x):
    return jax.nn.silu(x)

def _sigmoid(x):
    return jax.nn.sigmoid(x)

def _layernorm(x, axis=-1, eps=1e-05):
    m = jnp.mean(x, axis=axis, keepdims=True)
    v = jnp.var(x, axis=axis, keepdims=True)
    return (x - m) / jnp.sqrt(v + eps)

def _scatter_add(tgt, idx, src, axis=0):
    return tgt.at[idx].add(src)

def _segment_sum(src, seg, n):
    return jax.ops.segment_sum(src, seg, n)
kernel_name = 'mk_sandwich_d1_jaxref_r8_1482c4'

def setup_inputs(seed: int=0):
    np.random.seed(seed)
    _w = jnp.asarray

    def _L0_attn_setup():
        import jax, jax.numpy as jnp
        import numpy as np
        B, N, E = (2, 256, 256)
        H, D = (16, 128)
        BASE = 10000.0

        def rope(t, offset=0):
            d = t.shape[-1]
            pos = jnp.arange(t.shape[1], dtype=jnp.float32) + offset
            inv = BASE ** (-jnp.arange(0, d, 2, dtype=jnp.float32) / d)
            ang = pos[:, None] * inv[None, :]
            cos = jnp.cos(ang)[None, :, None, :]
            sin = jnp.sin(ang)[None, :, None, :]
            t1, t2 = (t[..., :d // 2], t[..., d // 2:])
            return jnp.concatenate([t1 * cos - t2 * sin, t2 * cos + t1 * sin], axis=-1)
        key = jax.random.key(seed)
        ks = jax.random.split(key, 6)
        s = lambda k, shape, fan: jax.random.normal(k, shape, jnp.float32) / np.sqrt(fan)
        return {'x': jax.random.normal(ks[0], (B, N, E), jnp.float32), 'Wq': s(ks[1], (H * D, E), E), 'Wkv': s(ks[2], (2 * D, E), E), 'Wkvh': s(ks[3], (2 * H, E), E), 'Wg': s(ks[4], (2 * H, E), E), 'Wout': s(ks[5], (E, H * D), H * D)}
    _L0_attn_in = _L0_attn_setup()

    def _L0_ffn_setup():
        import jax, jax.numpy as jnp
        import numpy as np
        GROUP_SIZE = 64

        def ternary_quant(w_fp32, g=GROUP_SIZE):
            w = w_fp32.astype(jnp.bfloat16)
            w_g = w.reshape(-1, g)
            scale = jnp.clip(jnp.mean(jnp.abs(w_g), axis=-1, keepdims=True), 1e-08, None)
            q = jnp.clip(jnp.round(w_g / scale), -1, 1)
            w_hat = (q * scale).reshape(w.shape)
            return w + jax.lax.stop_gradient(w_hat - w)

        def rms_norm(x):
            eps = jnp.finfo(x.dtype).eps.astype(jnp.float32)
            xf = x.astype(jnp.float32)
            inv = jax.lax.rsqrt(jnp.mean(xf * xf, axis=-1, keepdims=True) + eps)
            return (xf * inv).astype(x.dtype)
        key = jax.random.key(seed)
        k1, k2, k3 = jax.random.split(key, 3)
        B, S, D = (2, 256, 256)
        H = 4 * D
        x = jax.random.normal(k1, (B, S, D), dtype=jnp.float32).astype(jnp.bfloat16)
        w_gate_up = jax.random.normal(k2, (2 * H, D), dtype=jnp.float32) * 0.02
        w_proj = jax.random.normal(k3, (D, H), dtype=jnp.float32) * 0.02
        return {'x': x, 'w_gate_up': w_gate_up, 'w_proj': w_proj}
    _L0_ffn_in = _L0_ffn_setup()
    _d = {'L0_attn_x': _L0_attn_in['x'], 'L0_attn_Wq': _L0_attn_in['Wq'], 'L0_attn_Wkv': _L0_attn_in['Wkv'], 'L0_attn_Wkvh': _L0_attn_in['Wkvh'], 'L0_attn_Wg': _L0_attn_in['Wg'], 'L0_attn_Wout': _L0_attn_in['Wout'], 'L0_ffn_w_gate_up': _L0_ffn_in['w_gate_up'], 'L0_ffn_w_proj': _L0_ffn_in['w_proj']}
    _x0 = _d['L0_attn_x']
    _d['L0_attn_x'] = jax.random.normal(jax.random.fold_in(jax.random.key(seed), 1), (16, 256, 256), dtype=_x0.dtype)
    del _x0
    return _d

def reference(L0_attn_x, L0_attn_Wq, L0_attn_Wkv, L0_attn_Wkvh, L0_attn_Wg, L0_attn_Wout, L0_ffn_w_gate_up, L0_ffn_w_proj):

    def _L0_attn_ref(x, Wq, Wkv, Wkvh, Wg, Wout):
        import jax, jax.numpy as jnp
        import numpy as np
        B, N, E = (2, 256, 256)
        H, D = (16, 128)
        BASE = 10000.0

        def rope(t, offset=0):
            d = t.shape[-1]
            pos = jnp.arange(t.shape[1], dtype=jnp.float32) + offset
            inv = BASE ** (-jnp.arange(0, d, 2, dtype=jnp.float32) / d)
            ang = pos[:, None] * inv[None, :]
            cos = jnp.cos(ang)[None, :, None, :]
            sin = jnp.sin(ang)[None, :, None, :]
            t1, t2 = (t[..., :d // 2], t[..., d // 2:])
            return jnp.concatenate([t1 * cos - t2 * sin, t2 * cos + t1 * sin], axis=-1)
        b, n, _ = x.shape
        q = (x @ Wq.T).reshape(b, n, H, D)
        kv = x @ Wkv.T
        kv_head = x @ Wkvh.T
        g = x @ Wg.T
        log_f = jnp.concatenate([jnp.zeros((b, 1, 2 * H), jnp.float32), jax.nn.log_sigmoid(g)], axis=1)
        log_f_cumsum = jnp.cumsum(log_f, axis=1)[:, :-1]
        kv_head = kv_head * jnp.exp(log_f_cumsum)
        kv_head = jnp.cumsum(kv_head, axis=1)
        kp, vp = (kv[..., :D], kv[..., D:])
        kh, vh = (kv_head[..., :H], kv_head[..., H:])
        k = jnp.einsum('bnd,bnh->bnhd', kp, kh)
        v = jnp.einsum('bnd,bnh->bnhd', vp, vh)
        q = rope(q)
        k = rope(k)
        scale = 1.0 / np.sqrt(D)
        scores = jnp.einsum('bnhd,bmhd->bhnm', q, k) * scale
        mask = jnp.tril(jnp.ones((n, n), bool))
        scores = jnp.where(mask[None, None], scores, -jnp.inf)
        p = jax.nn.softmax(scores, axis=-1)
        o = jnp.einsum('bhnm,bmhd->bnhd', p, v).reshape(b, n, H * D)
        return o @ Wout.T

    def _L0_ffn_ref(x, w_gate_up, w_proj):
        import jax, jax.numpy as jnp
        import numpy as np
        GROUP_SIZE = 64

        def ternary_quant(w_fp32, g=GROUP_SIZE):
            w = w_fp32.astype(jnp.bfloat16)
            w_g = w.reshape(-1, g)
            scale = jnp.clip(jnp.mean(jnp.abs(w_g), axis=-1, keepdims=True), 1e-08, None)
            q = jnp.clip(jnp.round(w_g / scale), -1, 1)
            w_hat = (q * scale).reshape(w.shape)
            return w + jax.lax.stop_gradient(w_hat - w)

        def rms_norm(x):
            eps = jnp.finfo(x.dtype).eps.astype(jnp.float32)
            xf = x.astype(jnp.float32)
            inv = jax.lax.rsqrt(jnp.mean(xf * xf, axis=-1, keepdims=True) + eps)
            return (xf * inv).astype(x.dtype)
        wq_gu = ternary_quant(w_gate_up)
        gu = jnp.einsum('bsd,hd->bsh', x, wq_gu)
        gate, up = jnp.split(gu, 2, axis=-1)
        h = jax.nn.silu(gate) * up
        hn = rms_norm(h)
        wq_p = ternary_quant(w_proj)
        return jnp.einsum('bsh,dh->bsd', hn, wq_p)
    x = L0_attn_x
    x = x + _layernorm(_L0_attn_ref(_layernorm(x, axis=-1), L0_attn_Wq, L0_attn_Wkv, L0_attn_Wkvh, L0_attn_Wg, L0_attn_Wout), axis=-1)
    x = x + _layernorm(_L0_ffn_ref(_layernorm(x, axis=-1), L0_ffn_w_gate_up, L0_ffn_w_proj), axis=-1)
    return x

_drawn_inputs = setup_inputs


def setup_inputs(seed=0):
    import zlib

    import numpy as np

    out = dict(_drawn_inputs(seed))
    spreads = {}
    factors = {}
    for name, (base, spread) in spreads.items():
        noise = np.random.default_rng([zlib.crc32(name.encode()), seed]).standard_normal(out[name].shape)
        drawn = base * np.exp(spread * noise) if base else spread * noise
        out[name] = jnp.asarray(drawn.astype(out[name].dtype))
    for name, factor in factors.items():
        out[name] = (out[name] * factor).astype(out[name].dtype)
    return out
```

```python
from contextlib import ExitStack

import numpy as np
import concourse.bass as bass
from concourse import mybir

F32 = mybir.dt.float32
F32R = mybir.dt.float32r
BF16 = mybir.dt.bfloat16
ACT = mybir.ActivationFunctionType
ALU = mybir.AluOpType
AX = mybir.AxisListType

P = 128
BATCH, N, E = 16, 256, 256
H, D = 16, 128
FF = 4 * E
GROUP = 64
LN_EPS = 1e-5
RMS_EPS = float(np.finfo(np.float32).eps)
ROPE_BASE = 10000.0

NT = N // P
ET = E // P
TILES = BATCH * NT
HP = 2
PAIRS = H // HP
STEPS = BATCH * PAIRS
FT = FF // P
MASKED = -1e30
ARENA = 15840

LAG = dict(project=0, rope=1, score=2, softmax=3, turn=4, value=5, out=6)
DRAIN = LAG["out"] + 2

FRONT = dict(stats=0, norm=2, turn=2, keys=3, gates=3, decay=4, coef=4, weigh=4, sums=5,
             key_rope=5, store=6, values=5, turn_vh=6, copy_vh=7)
TAIL = dict(copy=5, stats=6, invert=6, norm=7, add=7)

FLAG = dict(stats=0, norm=1, turn=1, up=2, sum=3, down=3, z=3)
FDRAIN = FLAG["z"]
FLEAD = 6
FSTART = PAIRS + 3
FC = 2

WLAG = dict(load=0, cast=2, sum=3, compare=3, decide=3, scale=4, change=5, finish=5, turn=6)
CHUNKS = 6


def sandwich_kernel(nc, x, wq, wkv, wkvh, wg, wout, wgu, wproj, rope, out):
    ctx = ExitStack()
    with ctx:
        def sb(name, shape, dt=F32):
            return ctx.enter_context(nc.sbuf_tensor(name, shape, dt))

        def sem(name):
            return ctx.enter_context(nc.semaphore(name))

        X = sb("X", [P, TILES, E])
        wq_hi = sb("wq_hi", [P, ET, H, D], F32R)
        wq_lo = sb("wq_lo", [P, ET, H, D], F32R)
        wkv_hi = sb("wkv_hi", [P, ET, 2 * D], F32R)
        wkv_lo = sb("wkv_lo", [P, ET, 2 * D], F32R)
        whg_hi = sb("whg_hi", [P, ET, P], F32R)
        whg_lo = sb("whg_lo", [P, ET, P], F32R)
        wo_hi = sb("wo_hi", [P, H, E], F32R)
        wo_lo = sb("wo_lo", [P, H, E], F32R)
        tables = sb("tables", [P, 4, N])
        ident = sb("ident", [P, P])
        ident_bf = sb("ident_bf", [P, P], BF16)
        ones = sb("ones", [P, 1])
        minus_half = sb("minus_half", [P, NT])
        eps = sb("eps", [P, 1])
        cosq, sinq, cosk, sink = (tables[:, i, :] for i in range(4))

        xt_hi = [sb(f"xt_hi{i}", [P, ET, N], F32R) for i in range(2)]
        xt_lo = [sb(f"xt_lo{i}", [P, ET, N], F32R) for i in range(2)]
        vals_hi = [sb(f"vals_hi{i}", [P, NT, D], F32R) for i in range(2)]
        vals_lo = [sb(f"vals_lo{i}", [P, NT, D], F32R) for i in range(2)]
        vh_col = [sb(f"vh_col{i}", [P, NT, 2 * H]) for i in range(2)]
        o_hi_all = sb("o_hi", [P, 2, HP, N], F32R)
        o_lo_all = sb("o_lo", [P, 2, HP, N], F32R)
        o_hi = [o_hi_all[:, i, :, :] for i in range(2)]
        o_lo = [o_lo_all[:, i, :, :] for i in range(2)]

        pt_f32 = sb("pt", [P, 2, 6 * P])
        pt_split = sb("pt_split", [P, 2, 2, 6 * P], F32R)
        pt = [pt_f32[:, i, :] for i in range(2)]
        pt_hi, pt_lo = ([pt_split[:, j, i, :] for i in range(2)] for j in range(2))
        arena = sb("arena", [P, ARENA])
        used = [0]

        def carve(*shape):
            n = int(np.prod(shape))
            a = arena[:, used[0]:used[0] + n]
            used[0] += n
            assert used[0] <= ARENA
            if len(shape) == 2:
                a = a.rearrange("p (a b) -> p a b", b=shape[1])
            return a

        rope_at = used[0]
        q_rot = [carve(HP, N) for _ in range(2)]
        q_cos = [carve(HP, N) for _ in range(2)]
        q_swap = [carve(HP, N) for _ in range(2)]
        kh_all = [carve(HP, N) for _ in range(4)]
        y_at = used[0]
        y_sb = carve(NT, E)
        y_norm = carve(NT, E)
        T_at = used[0]
        T = [carve(6 * P) for _ in range(4)]
        front_at_word = used[0]
        xn = carve(NT, E)
        k_cos, k_swap = carve(N), carve(N)
        gate_e = carve(N)
        decay = carve(N)
        coef = carve(N)
        kvw = carve(N)
        kv_cum = [carve(N) for _ in range(2)]
        small = carve(96)
        w_stage_at = used[0]
        w_stage = [carve(FF) for _ in range(2)]
        w_signs1, w_bf2 = carve(FF // 2), carve(FF // 2)
        keys_at = used[0]
        keys = [carve(N) for _ in range(2)][::-1]
        carve(N)
        w_small = carve(64)
        small3 = carve(64)

        used[0] = y_at
        stage_kv = carve(2, E)
        stage_hg = carve(E)
        QF = 4
        stage_q0 = pt_f32[:, :, :].rearrange("p a c -> p (a c)")[:, 0:QF * E].rearrange("p (h e) -> p h e", e=E)
        used[0] = w_stage_at
        stage_q1 = carve(H - QF, E)
        assert used[0] <= keys_at
        stage_o = X[:, TILES // 2:, :].rearrange("p t e -> p (t e)").rearrange("p (t c) -> p t c", t=ET)

        wgu_t = wq_hi[:, :, :, :].rearrange("p k h d -> p k (h d)")
        wpr_t = wq_lo[:, 0, :, :].rearrange("p h d -> p (h d)").rearrange("p (f e) -> p f e", e=E)
        used[0] = front_at_word
        w_other = carve(FF // 2).bitcast(BF16)
        w_bf = [carve(FF // 2).bitcast(BF16) for _ in range(2)] + [w_bf2.bitcast(BF16)]
        w_signs = [carve(FF // 2).bitcast(BF16), w_signs1.bitcast(BF16)]
        used[0] = keys_at + N
        w_tern = [tables[:, 2:4, :].rearrange("p a n -> p (a n)").bitcast(BF16), carve(FF // 2).bitcast(BF16)]
        w_sums, w_half = w_small[:, 0:16], w_small[:, 16:24].bitcast(BF16)
        w_scale = [w_small[:, 24 + 8 * i:32 + 8 * i].bitcast(BF16) for i in range(2)]

        used[0] = rope_at
        hid = [carve(FT, N) for _ in range(2)]
        x2n = [carve(NT, E) for _ in range(2)]
        assert used[0] <= y_at
        used[0] = T_at
        sig = [carve(FC * N) for _ in range(2)]
        z = [carve(NT, E) for _ in range(2)]
        zn = [carve(NT, E) for _ in range(2)]
        assert used[0] <= front_at_word
        used[0] = front_at_word
        squares = [carve(FT, N)]
        sums = [carve(N) for _ in range(2)]
        used[0] = w_stage_at
        squares.append(carve(FT, N))
        res = [pt_f32[:, :, :].rearrange("p a c -> p (a c)")[:, i * NT * E:(i + 1) * NT * E].rearrange("p (t e) -> p t e", e=E)
               for i in range(2)]
        x2_hi, x2_lo = xt_hi, xt_lo
        ht_hi, ht_lo = ([w[:, i * FT:(i + 1) * FT, :] for i in range(2)] for w in (wo_hi, wo_lo))

        nmax = [small[:, 4 * i:4 * i + 4] for i in range(4)]
        rsum = [small[:, 16 + 4 * i:20 + 4 * i] for i in range(4)]
        rinv = [small[:, 32 + 4 * i:36 + 4 * i] for i in range(4)]
        ln1_stat = small[:, 48:60].rearrange("p (t a) -> p t a", a=6)
        ln1_agg = small[:, 60:64].rearrange("p (t a) -> p t a", a=2)
        ln1_rstd = small[:, 64:66]
        ln2_stat = small[:, 66:78].rearrange("p (t a) -> p t a", a=6)
        ln2_agg = small[:, 78:82].rearrange("p (t a) -> p t a", a=2)
        ln2_rstd = small[:, 82:84]

        x2_stat = small3[:, 0:12].rearrange("p (t a) -> p t a", a=6)
        x2_agg = small3[:, 12:16].rearrange("p (t a) -> p t a", a=2)
        x2_rstd = small3[:, 16:18]
        z_stat = small3[:, 18:30].rearrange("p (t a) -> p t a", a=6)
        z_agg = small3[:, 30:34].rearrange("p (t a) -> p t a", a=2)
        z_rstd = small3[:, 34:36]
        rms = [small3[:, 36 + 2 * i:38 + 2 * i] for i in range(2)]

        kh_dram = nc.dram_tensor("kh_rows", [BATCH, H, N], F32, kind="Internal").ap()

        psum = ctx.enter_context(nc.psum_tensor("psum", [P, 8, 512], F32))
        bank = [psum[:, i, :] for i in range(8)]
        Q_BANK, S1_BANK, S0_BANK, PT0_BANK, PT1_BANK, O_BANK, Y_BANK, F_BANK = bank
        heads = lambda ap, n: ap.rearrange("p (h n) -> p h n", n=n)

        consts = sem("consts")
        zeroed = sem("zeroed")
        tables_in = sem("tables_in")
        x_first, x_second, x_half, x_rest = (sem(f"x_{k}") for k in ("first", "second", "half", "rest"))
        w_in = {k: sem(f"w_in_{k}") for k in ("q0", "q1", "kv", "hg", "o")}
        w_turned, w_hi_done, w_lo_done = sem("w_turned"), sem("w_hi_done"), sem("w_lo_done")
        ln1_stats, ln1_aggr, ln1_eps, ln1_inv, ln1_done = (
            sem(f"ln1_{k}") for k in ("stats", "aggr", "eps", "inv", "done"))
        xt_turned, xt_hi_done, xt_lo_done = sem("xt_turned"), sem("xt_hi_done"), sem("xt_lo_done")
        kg_ready, k_swapped, k_cos_done, k_sin_done, k_ready = (
            sem(k) for k in ("kg_ready", "k_swapped", "k_cos_done", "k_sin_done", "k_ready"))
        gate_exp, gate_one, decay_done, coef_done, kvw_done, cum_done = (
            sem(k) for k in ("gate_exp", "gate_one", "decay_done", "coef_done", "kvw_done", "cum_done"))
        v_ready, v_hi_done, v_lo_done, vh_turned, vh_copied = (
            sem(k) for k in ("v_ready", "v_hi_done", "v_lo_done", "vh_turned", "vh_copied"))
        kh_stored = sem("kh_stored")
        y_copied, ln2_stats, ln2_aggr, ln2_eps, ln2_inv = (
            sem(k) for k in ("y_copied", "ln2_stats", "ln2_aggr", "ln2_eps", "ln2_inv"))
        ln2_done, x1_done = sem("ln2_done"), sem("x1_done")
        q_ready, q_swapped, q_cosined, q_sined, q_roped = (
            sem(k) for k in ("q_ready", "q_swapped", "q_cosined", "q_sined", "q_roped"))
        kh_in = [sem(f"kh_in{i}") for i in range(4)]
        s_ready, s_weighted, s_masked, s_max, p_exp, p_inv, p_ready = (
            sem(k) for k in ("s_ready", "s_weighted", "s_masked", "s_max", "p_exp", "p_inv", "p_ready"))
        pt_ready, pt_weighted, pt_hi_done, pt_lo_done, o_ready, o_hi_done, o_lo_done, y_added = (
            sem(k) for k in ("pt_ready", "pt_weighted", "pt_hi_done", "pt_lo_done", "o_ready", "o_hi_done", "o_lo_done",
                             "y_added"))
        wt_in = [sem(f"wt_in{i}") for i in range(2)]
        wt_cast, wt_summed, wt_scaled, wt_compared, wt_decided, wt_signed, wt_changed, wt_done, wt_turned, wt_copied = (
            sem(f"wt_{k}") for k in ("cast", "summed", "scaled", "compared", "decided", "signed", "changed", "done",
                                     "turned", "copied"))
        x2_stats, x2_aggr, x2_eps, x2_inv, x2_norm, x2_turned, x2_hi_done, x2_lo_done = (
            sem(f"x2_{k}") for k in ("stats", "aggr", "eps", "inv", "norm", "turned", "hi_done", "lo_done"))
        gate_ready, up_ready, gate_silu, h_ready, h_squared, ht_hi_done, ht_lo_done = (
            sem(k) for k in ("gate_ready", "up_ready", "gate_silu", "h_ready", "h_squared", "ht_hi_done", "ht_lo_done"))
        h_summed, sum_ready, rms_eps, rms_done, z_ready = (
            sem(k) for k in ("h_summed", "sum_ready", "rms_eps", "rms_done", "z_ready"))
        z_scaled, z_stats, z_aggr, z_eps, z_inv, z_norm, res_done = (
            sem(k) for k in ("z_scaled", "z_stats", "z_aggr", "z_eps", "z_inv", "z_norm", "res_done"))
        stored = [sem(f"stored{i}") for i in range(2)]

        block = ctx.enter_context(nc.Block())

        def at_least(eng, s, value):
            if not (isinstance(value, int) and value <= 0):
                eng.wait_ge(s, value)

        def pair_at(g0, s, lag):
            g = g0 + (s - lag)
            if isinstance(g0, int) and not 0 <= g < STEPS:
                return None
            return g, (s - lag) % PAIRS, s < lag

        def front_at(g0, s, stage):
            if s == FRONT[stage] and not (isinstance(g0, int) and g0 + PAIRS >= STEPS):
                return g0 + PAIRS

        def tail_at(g0, s, stage):
            if s == TAIL[stage] and not (isinstance(g0, int) and g0 == 0):
                return g0 - PAIRS

        def in_last_batch(g):
            return isinstance(g, int) and g >= STEPS - PAIRS

        def chunk_at(g0, s, stage):
            if isinstance(g0, int):
                c = g0 + s - (STEPS - PAIRS) - WLAG[stage]
                if 0 <= c < CHUNKS:
                    return c

        def over_batches(eng, batch):
            batch(0, 0, PAIRS)
            with eng.Fori(PAIRS, STEPS - 3 * PAIRS + 1, 2 * PAIRS) as g0:
                batch(g0, 1, PAIRS)
                batch(g0 + PAIRS, 0, PAIRS)
            batch(STEPS - PAIRS, 1, PAIRS)
            batch(STEPS, 0, DRAIN)

        def unit_at(u0, s, lag):
            u = u0 + (s - lag)
            if isinstance(u0, int) and not 0 <= u < BATCH:
                return None
            return u, (s - lag) % 2

        def early_unit_step(g0, s, step):
            if isinstance(g0, int) and g0 + s >= STEPS - PAIRS + FSTART:
                step(0, g0 + s - (STEPS - PAIRS + FSTART))

        def over_units(eng, step):
            for s in range(PAIRS + DRAIN - FSTART, FLEAD):
                step(0, s)
            with eng.Fori(FLEAD, BATCH - 1, 2) as u:
                for s in range(2):
                    step(u, s)
            for s in range(FDRAIN):
                step(BATCH, s)

        def x_tiles(g0):
            return x_batch(g0, NT * E // PAIRS)

        def x_batch(u, size=NT * E):
            flat = X[:, :, :].rearrange("p t e -> p (t e)")
            return flat[:, bass.ds(u * size, NT * E)].rearrange("p (t e) -> p t e", e=E)

        turns = [("kv", wkv_hi, wkv_lo, 0, 0), ("hg", whg_hi, whg_lo, 1, 0)]
        turns += [(("q", 2 * i), wq_hi, wq_lo, 3 + i % 4, i - 1 if i > 3 else 0) for i in range(H // 2)]
        LATER, LATER_A_STEP = 2 + QF // 2, 3
        turns += [(("o", 2 * i), wo_hi, wo_lo, 3 + (H // 2 + i) % 4, H // 2 + i - 1) for i in range(H // 2)]

        def turn_target(what, w):
            if what == "kv":
                return w[:, :, :], lambda b: b.rearrange("p (k c) -> p k c", k=ET)
            if what == "hg":
                return w[:, :, 0:4 * H], lambda b: b[:, 0:ET * 4 * H].rearrange("p (k c) -> p k c", k=ET)
            kind, h = what
            if kind == "q":
                return w[:, :, h:h + 2, :], lambda b: b.rearrange("p (k h d) -> p k h d", k=ET, h=2)
            return w[:, h:h + 2, :], lambda b: b.rearrange("p (h e) -> p h e", h=2)

        def later_turns(g0, s):
            if isinstance(g0, int) and g0 == 0:
                i = LATER + s * LATER_A_STEP
                return range(i, min(i + LATER_A_STEP, len(turns)))
            return ()

        @block.sync
        def _(sp):
            tile_rows = x.rearrange("b (t p) e -> p (b t) e", p=P)
            half = TILES // 2
            sp.dma_start(X[:, 0:NT, :], tile_rows[:, 0:NT, :]).then_inc(x_first, 16)
            sp.dma_start(stage_kv, wkv.rearrange("(t p) e -> p t e", p=P)).then_inc(w_in["kv"], 16)
            sp.dma_start(stage_hg[0:2 * H, :], wkvh).then_inc(w_in["hg"], 16)
            sp.dma_start(stage_hg[2 * H:4 * H, :], wg).then_inc(w_in["hg"], 16)
            q_rows = wq.rearrange("(t p) e -> p t e", p=P)
            sp.dma_start(stage_q0, q_rows[:, 0:QF, :]).then_inc(w_in["q0"], 16)
            sp.dma_start(tables[:, :, :], rope).then_inc(tables_in, 16)
            sp.dma_start(X[:, NT:2 * NT, :], tile_rows[:, NT:2 * NT, :]).then_inc(x_second, 16)
            sp.dma_start(stage_q1, q_rows[:, QF:H, :]).then_inc(w_in["q1"], 16)
            sp.dma_start(stage_o, wout.rearrange("(t p) c -> p t c", p=P)).then_inc(w_in["o"], 16)
            sp.dma_start(X[:, 2 * NT:half, :], tile_rows[:, 2 * NT:half, :]).then_inc(x_half, 16)

            kh_flat = kh_dram.rearrange("b h n -> (b h n)")
            gu_rows = wgu.rearrange("(c t p) e -> c p t e", p=P, t=FF // E)
            pr_rows = wproj.rearrange("(c p) f -> c p f", p=P)

            def address(value):
                return value if isinstance(value, int) else sp.snap(value)

            def store_kh(c0, par):
                row = kh_flat[bass.ds(address(c0 * (H * N // PAIRS)), H * N)]
                sp.wait_ge(cum_done, c0 + PAIRS)
                sp.dma_start(row.rearrange("(h n) -> h n", n=N), kv_cum[par][0:H, :]).then_inc(kh_stored, 16)

            def spread_kh(g0, par, s):
                at = pair_at(g0, s, LAG["project"])
                if at:
                    g, p, _ = at
                    row = kh_flat[bass.ds(address(g0 * (H * N // PAIRS) + p * HP * N), HP * N)]
                    at_least(sp, s_weighted, g - 3)
                    if p == 0:
                        sp.wait_ge(kh_stored, g0 * (16 // PAIRS) + 16)
                    sp.dma_start(kh_all[p % 4], row.rearrange("(h n) -> h n", n=N).partition_broadcast(P))\
                      .then_inc(kh_in[p % 4], 16)

            def batch(g0, par, steps):
                for s in range(steps):
                    c = chunk_at(g0, s, "load")
                    if c is not None:
                        at_least(sp, wt_cast, c - 1)
                        if c < CHUNKS - ET:
                            sp.dma_start(w_stage[c % 2].rearrange("p (t e) -> p t e", e=E), gu_rows[c])\
                              .then_inc(wt_in[c % 2], 16)
                        else:
                            sp.dma_start(w_stage[c % 2], pr_rows[c - (CHUNKS - ET)]).then_inc(wt_in[c % 2], 16)
                    spread_kh(g0, par, s)
                    c0 = front_at(g0, s, "store")
                    if c0 is not None:
                        store_kh(c0, 1 - par)
                    if isinstance(g0, int) and g0 == 0 and s == 4:
                        sp.wait_ge(w_turned, len(turns))
                        sp.dma_start(X[:, half:TILES, :], tile_rows[:, half:TILES, :]).then_inc(x_rest, 16)

            store_kh(0, 0)
            over_batches(sp, batch)

            out_rows = out.rearrange("b (t p) e -> p (b t) e", p=P)
            with sp.Fori(0, BATCH - 1, 2) as u:
                for i in range(2):
                    rows = out_rows[:, bass.ds(address((u + i) * NT), NT), :]
                    sp.wait_ge(res_done, u + i + 1)
                    sp.dma_start(rows, res[i]).then_inc(stored[i], 16)
            for i in range(2):
                sp.wait_ge(stored[i], 16 * BATCH // 2)

        @block.gpsimd
        def _(pool):
            nc.gpsimd.memset(minus_half[:, :], -0.5).then_inc(zeroed, 1)
            nc.gpsimd.memset(ident[:, :], 0.0).then_inc(zeroed, 1)
            nc.gpsimd.memset(ident_bf[:, :], 0.0).then_inc(zeroed, 1)
            nc.gpsimd.memset(eps[:, :], LN_EPS).then_inc(zeroed, 1)
            pool.wait_ge(zeroed, 4)
            for m in (ident, ident_bf):
                nc.gpsimd.affine_select(out=m[:, :], in_=m[:, :], compare_op=ALU.not_equal, fill=1.0, base=0,
                                        pattern=[[-1, P]], channel_multiplier=1).then_inc(consts, 1)
            masked_fill = pool.to_reg(MASKED)

            def invert_x(c0):
                pool.wait_ge(ln1_aggr, c0 + PAIRS)
                at_least(pool, ln1_done, c0)
                nc.gpsimd.tensor_tensor(ln1_rstd, ln1_agg[:, :, 1], eps[:, 0:1].to_broadcast([P, NT]), ALU.add)\
                    .then_inc(ln1_eps, PAIRS)
                pool.wait_ge(ln1_eps, c0 + PAIRS)
                nc.gpsimd.tensor_tensor(ln1_rstd, ln1_rstd, minus_half[:, 0:NT], ALU.pow).then_inc(ln1_inv, PAIRS)

            def key_rope(c0, par):
                pool.wait_ge(k_swapped, c0 + PAIRS)
                nc.gpsimd.tensor_tensor(k_swap, k_swap, sink, ALU.mult).then_inc(k_sin_done, PAIRS)
                pool.wait_ge(k_sin_done, c0 + PAIRS)
                pool.wait_ge(k_cos_done, c0 + PAIRS)
                at_least(pool, s_ready, c0 - PAIRS)
                nc.gpsimd.tensor_tensor(keys[par], k_cos, k_swap, ALU.add).then_inc(k_ready, PAIRS)

            def invert_y(c0):
                pool.wait_ge(ln2_aggr, c0 + PAIRS)
                nc.gpsimd.tensor_tensor(ln2_rstd, ln2_agg[:, :, 1], eps[:, 0:1].to_broadcast([P, NT]), ALU.add)\
                    .then_inc(ln2_eps, PAIRS)
                pool.wait_ge(ln2_eps, c0 + PAIRS)
                nc.gpsimd.tensor_tensor(ln2_rstd, ln2_rstd, minus_half[:, 0:NT], ALU.pow).then_inc(ln2_inv, PAIRS)

            def residual(c0):
                pool.wait_ge(ln2_done, c0 + 2 * PAIRS)
                xs = x_tiles(c0)
                nc.gpsimd.tensor_tensor(xs, xs, y_norm, ALU.add).then_inc(x1_done, PAIRS)

            def queries_sin(g0, s):
                at = pair_at(g0, s, LAG["rope"])
                if at:
                    g, p, _ = at
                    swap, spread = q_swap[p % 2], sinq.unsqueeze(1).to_broadcast([P, HP, N])
                    pool.wait_ge(q_swapped, g + 1)
                    nc.gpsimd.tensor_tensor(swap, swap, spread, ALU.mult).then_inc(q_sined, 1)

            def queries_add(g0, s):
                at = pair_at(g0, s, LAG["rope"])
                if at:
                    g, p, _ = at
                    pool.wait_ge(q_sined, g + 1)
                    pool.wait_ge(q_cosined, g + 1)
                    at_least(pool, s_ready, g - 1)
                    nc.gpsimd.tensor_tensor(q_rot[p % 2], q_cos[p % 2], q_swap[p % 2], ALU.add).then_inc(q_roped, 1)

            def mask(g0, s):
                at = pair_at(g0, s, LAG["score"])
                if at:
                    g, p, _ = at
                    diag = heads(T[p % 4][:, 2 * P:6 * P], P)
                    pool.wait_ge(s_weighted, g + 1)
                    nc.gpsimd.affine_select(out=diag, in_=diag, compare_op=ALU.is_ge, fill=masked_fill, base=0,
                                            pattern=[[0, 2 * HP], [-1, P]], channel_multiplier=1).then_inc(s_masked, 2)

            def split_pt(g0, s):
                at = pair_at(g0, s, LAG["turn"])
                if at:
                    g, p, _ = at
                    pool.wait_ge(pt_hi_done, g + 1)
                    nc.gpsimd.tensor_tensor(pt_lo[p % 2], pt[p % 2], pt_hi[p % 2].bitcast(F32), ALU.subtract)\
                        .then_inc(pt_lo_done, 1)

            def weights_scale(g0, s):
                c = chunk_at(g0, s, "scale")
                if c is not None:
                    q, spread = w_signs[c % 2], w_scale[c % 2].unsqueeze(2).to_broadcast([P, FF // GROUP, GROUP])
                    pool.wait_ge(wt_decided, c + 1)
                    nc.gpsimd.tensor_tensor(heads(q, GROUP), heads(q, GROUP), spread, ALU.mult).then_inc(wt_signed, 1)

            def split_hidden(u, i, c):
                tiles = slice(c * FC, (c + 1) * FC)
                pool.wait_ge(ht_hi_done, u * (FT // FC) + (c + 1))
                nc.gpsimd.tensor_tensor(ht_lo[i][:, tiles, :], hid[i][:, tiles, :], ht_hi[i][:, tiles, :].bitcast(F32),
                                        ALU.subtract).then_inc(ht_lo_done, 1)

            def step(u0, s):
                at = unit_at(u0, s, FLAG["up"])
                if at:
                    split_hidden(*at, 0)
                at = unit_at(u0, s, FLAG["stats"])
                if at:
                    u, i = at
                    pool.wait_ge(x2_aggr, u * 2 * NT + 2 * NT)
                    at_least(pool, x2_norm, u * NT)
                    nc.gpsimd.tensor_tensor(x2_rstd, x2_agg[:, :, 1], eps[:, :].to_broadcast([P, NT]), ALU.add)\
                        .then_inc(x2_eps, 1)
                at = unit_at(u0, s, FLAG["stats"])
                if at:
                    u, i = at
                    pool.wait_ge(x2_eps, u + 1)
                    nc.gpsimd.tensor_tensor(x2_rstd, x2_rstd, minus_half[:, 0:NT], ALU.pow).then_inc(x2_inv, 1)
                at = unit_at(u0, s, FLAG["down"])
                if at:
                    u, i = at
                    pool.wait_ge(rms_eps, u + 1)
                    nc.gpsimd.tensor_tensor(rms[i], rms[i], minus_half[:, 0:NT], ALU.pow).then_inc(rms_done, 1)
                at = unit_at(u0, s, FLAG["up"])
                if at:
                    split_hidden(*at, 1)
                at = unit_at(u0, s, FLAG["up"])
                if at:
                    split_hidden(*at, 2)
                at = unit_at(u0, s, FLAG["z"])
                if at:
                    u, i = at
                    pool.wait_ge(z_aggr, u * 2 * NT + 2 * NT)
                    at_least(pool, z_norm, u * NT)
                    nc.gpsimd.tensor_tensor(z_rstd, z_agg[:, :, 1], eps[:, :].to_broadcast([P, NT]), ALU.add)\
                        .then_inc(z_eps, 1)
                at = unit_at(u0, s, FLAG["z"])
                if at:
                    u, i = at
                    pool.wait_ge(z_eps, u + 1)
                    nc.gpsimd.tensor_tensor(z_rstd, z_rstd, minus_half[:, 0:NT], ALU.pow).then_inc(z_inv, 1)
                at = unit_at(u0, s, FLAG["up"])
                if at:
                    split_hidden(*at, 3)
                at = unit_at(u0, s, FLAG["z"])
                if at:
                    u, i = at
                    pool.wait_ge(z_norm, u * NT + NT)
                    at_least(pool, stored[i], (u - i) * 8)
                    nc.gpsimd.tensor_tensor(res[i], zn[i], x_batch(u), ALU.add).then_inc(res_done, 1)

            def batch(g0, par, steps):
                for s in range(steps):
                    queries_sin(g0, s)
                    mask(g0, s)
                    queries_add(g0, s)
                    c0 = tail_at(g0, s, "invert")
                    if c0 is not None:
                        invert_y(c0)
                    split_pt(g0, s)
                    c0 = tail_at(g0, s, "add")
                    if c0 is not None:
                        residual(c0)
                    weights_scale(g0, s)
                    c0 = front_at(g0, s, "key_rope")
                    if c0 is not None:
                        key_rope(c0, 1 - par)
                    early_unit_step(g0, s, step)
                    c0 = front_at(g0, s, "stats")
                    if c0 is not None:
                        invert_x(c0)

            invert_x(0)
            pool.wait_ge(tables_in, 16)
            key_rope(0, 0)
            over_batches(pool, batch)
            over_units(pool, step)

        @block.tensor
        def _(pe):
            def three_passes(o, pairs_hi_lo, start=True, stop=True, skip=False):
                passes = [ab for ah, al, bh, bl in pairs_hi_lo for ab in ((ah, bh), (ah, bl), (al, bh))]
                for i, (a, b) in enumerate(passes):
                    last = nc.tensor.matmul(o, a, b, start=start and i == 0, stop=stop and i == len(passes) - 1,
                                            skip_group_check=skip)
                return last

            def turn_weight(i):
                what, _, _, b, left = turns[i]
                kind = what if isinstance(what, str) else what[0]
                at_least(pe, w_lo_done, left)
                came = ("q0" if what[1] < QF else "q1") if kind == "q" else kind
                pe.wait_ge(w_in[came], 32 if kind == "hg" else 16)
                b = bank[b]
                if kind == "kv":
                    blocks = [(b[:, (k * 2 + t) * P:(k * 2 + t + 1) * P], stage_kv[:, t, k * P:(k + 1) * P])
                              for k in range(ET) for t in range(2)]
                elif kind == "hg":
                    blocks = [(b[:, k * 4 * H:(k + 1) * 4 * H], stage_hg[0:4 * H, k * P:(k + 1) * P]) for k in range(ET)]
                elif kind == "q":
                    stage, first = (stage_q0, what[1]) if what[1] < QF else (stage_q1, what[1] - QF)
                    blocks = [(b[:, (k * 2 + j) * P:(k * 2 + j + 1) * P], stage[:, first + j, k * P:(k + 1) * P])
                              for k in range(ET) for j in range(2)]
                else:
                    blocks = [(b[:, (j * ET + t) * P:(j * ET + t + 1) * P],
                               stage_o[:, t, (what[1] + j) * D:(what[1] + j + 1) * D])
                              for j in range(2) for t in range(ET)]
                for o, i_ in blocks:
                    n = i_.shape[0]
                    last = nc.tensor.transpose(o, i_, ident[0:n, 0:n])
                last.then_inc(w_turned, 1)

            def turn_x(c0, par):
                pe.wait_ge(ln1_done, c0 + PAIRS)
                at_least(pe, vh_copied, c0)
                for k in range(ET):
                    for t in range(NT):
                        last = nc.tensor.transpose(F_BANK[:, k * N + t * P:k * N + (t + 1) * P],
                                                   xn[:, t, k * P:(k + 1) * P], ident[:, :])
                last.then_inc(xt_turned, PAIRS)

            def project_keys(c0, par):
                pe.wait_ge(xt_lo_done, c0 + PAIRS)
                xs = [(xt_hi[par][:, k, :], xt_lo[par][:, k, :]) for k in range(ET)]
                three_passes(F_BANK[:, 0:N], [(wkv_hi[:, k, 0:D], wkv_lo[:, k, 0:D], *xs[k]) for k in range(ET)])
                three_passes(F_BANK[:, N:2 * N], [(whg_hi[:, k, :], whg_lo[:, k, :], *xs[k]) for k in range(ET)])\
                    .then_inc(kg_ready, PAIRS)

            def project_values(c0, par):
                pe.wait_ge(kvw_done, c0 + PAIRS)
                for t in range(NT):
                    last = three_passes(F_BANK[:, t * D:(t + 1) * D], [
                        (xt_hi[par][:, k, t * P:(t + 1) * P], xt_lo[par][:, k, t * P:(t + 1) * P],
                         wkv_hi[:, k, D:2 * D], wkv_lo[:, k, D:2 * D]) for k in range(ET)])
                last.then_inc(v_ready, PAIRS)

            def turn_vh(c0, par):
                pe.wait_ge(cum_done, c0 + PAIRS)
                pe.wait_ge(v_lo_done, c0 + PAIRS)
                for t in range(NT):
                    last = nc.tensor.matmul(F_BANK[:, t * 2 * H:(t + 1) * 2 * H], kv_cum[par][0:2 * H, t * P:(t + 1) * P],
                                            ident[0:2 * H, 0:2 * H], start=True, stop=True)
                last.then_inc(vh_turned, PAIRS)

            def project(g0, par, s):
                at = pair_at(g0, s, LAG["project"])
                if at:
                    g, p, _ = at
                    if p == 0:
                        pe.wait_ge(xt_lo_done, g0 + PAIRS)
                    if isinstance(g0, int) and g0 == 0:
                        pe.wait_ge(w_lo_done, 3 + p)
                    at_least(pe, q_cosined, g)
                    for j in range(HP):
                        h = p * HP + j
                        last = three_passes(Q_BANK[:, j * N:(j + 1) * N],
                                            [(wq_hi[:, k, h, :], wq_lo[:, k, h, :], xt_hi[par][:, k, :],
                                              xt_lo[par][:, k, :]) for k in range(ET)])
                    last.then_inc(q_ready, 1)

            def score(g0, par, s):
                at = pair_at(g0, s, LAG["score"])
                if at:
                    g, p, back = at
                    kt = keys[par ^ back]
                    pe.wait_ge(q_roped, g + 1)
                    if p == 0:
                        pe.wait_ge(k_ready, (g0 - PAIRS if back else g0) + PAIRS)
                    at_least(pe, s_weighted, g)
                    for j in range(HP):
                        o = S1_BANK.rearrange("p (t h m) -> p t h m", t=NT, h=HP)[:, :, j, :]
                        nc.tensor.matmul(o, q_rot[p % 2][:, j, P:N], kt[:, :], start=True, stop=True, skip_group_check=True)
                        last = nc.tensor.matmul(S0_BANK[:, j * P:(j + 1) * P], q_rot[p % 2][:, j, 0:P], kt[:, 0:P],
                                                start=True, stop=True, skip_group_check=True)
                    last.then_inc(s_ready, 1)

            def turn(g0, par, s):
                at = pair_at(g0, s, LAG["turn"])
                if at:
                    g, p, _ = at
                    tb = T[p % 4]
                    pe.wait_ge(p_ready, g + 1)
                    if isinstance(g0, int) and g == 0:
                        pe.wait_ge(w_lo_done, len(turns) - 2)
                    at_least(pe, pt_weighted, g)
                    for j in range(HP):
                        nc.tensor.transpose(PT0_BANK[:, j * N:j * N + P], tb[:, (4 + j) * P:(5 + j) * P], ident[:, :])
                        nc.tensor.transpose(PT0_BANK[:, j * N + P:(j + 1) * N], tb[:, j * P:(j + 1) * P], ident[:, :])
                        last = nc.tensor.transpose(PT1_BANK[:, j * P:(j + 1) * P], tb[:, (2 + j) * P:(3 + j) * P],
                                                   ident[:, :])
                    last.then_inc(pt_ready, 1)

            def value(g0, par, s):
                at = pair_at(g0, s, LAG["value"])
                if at:
                    g, p, back = at
                    vh, vl, ph, pl = vals_hi[par ^ back], vals_lo[par ^ back], pt_hi[p % 2], pt_lo[p % 2]
                    pe.wait_ge(pt_lo_done, g + 1)
                    if p == 0:
                        pe.wait_ge(v_lo_done, (g0 - PAIRS if back else g0) + PAIRS)
                    if isinstance(g0, int) and g == 0:
                        pe.wait_ge(w_lo_done, len(turns) - 1)
                    at_least(pe, o_lo_done, g)
                    first, second = slice(0, 4 * P), slice(4 * P, 6 * P)
                    three_passes(O_BANK, [(vh[:, 0, :], vl[:, 0, :], ph[:, first], pl[:, first])], stop=False, skip=True)
                    three_passes(heads(O_BANK, N)[:, :, P:N], [(vh[:, 1, :], vl[:, 1, :], ph[:, second], pl[:, second])],
                                 start=False, skip=True).then_inc(o_ready, 1)

            def project_out(g0, par, s):
                at = pair_at(g0, s, LAG["out"])
                if at:
                    g, p, back = at
                    pe.wait_ge(o_lo_done, g + 1)
                    if p == 0:
                        at_least(pe, y_copied, g0 - PAIRS if back else g0)
                    if isinstance(g0, int) and g < H // HP:
                        pe.wait_ge(w_lo_done, len(turns))
                    for j in range(HP):
                        h = p * HP + j
                        for t in range(NT):
                            ts = slice(t * P, (t + 1) * P)
                            last = three_passes(Y_BANK[:, t * E:(t + 1) * E],
                                                [(o_hi[p % 2][:, j, ts], o_lo[p % 2][:, j, ts], wo_hi[:, h, :],
                                                  wo_lo[:, h, :])],
                                                start=h == 0 and t == 0, skip=True)
                    last.then_inc(y_added, 1)

            def weights_turn(g0, s):
                c = chunk_at(g0, s, "turn")
                if c is not None:
                    b = F_BANK.bitcast(BF16)
                    pe.wait_ge(wt_done, c + 1)
                    pe.wait_ge(vh_copied, STEPS)
                    at_least(pe, wt_copied, c)
                    for a in range(FF // P):
                        last = nc.tensor.transpose(b[:, a * P:(a + 1) * P], w_tern[c % 2][:, a * P:(a + 1) * P],
                                                   ident_bf[:, :])
                    last.then_inc(wt_turned, 1)

            def up(u, i, c):
                if c == 0:
                    pe.wait_ge(x2_lo_done, u + 1)
                if isinstance(u, int) and u == 0 and c == 0:
                    pe.wait_ge(pt_weighted, STEPS)
                for half, gone in enumerate((gate_silu, h_ready)):
                    at_least(pe, gone, u * (FT // FC) + (c - 1))
                    for j in range(FC):
                        col = half * FF + (c * FC + j) * P
                        parts = [(k, part[i]) for k in range(ET) for part in (x2_hi, x2_lo)]
                        for n, (k, part) in enumerate(parts):
                            last = nc.tensor.matmul(bank[c % 2 * 2 + half][:, j * N:(j + 1) * N], wgu_t[:, k, col:col + P],
                                                    part[:, k, :], start=n == 0 and j == 0, stop=n == len(parts) - 1,
                                                    skip_group_check=True)
                    last.then_inc((gate_ready, up_ready)[half], 1)

            def down(u, i):
                for c in range(FT // FC):
                    pe.wait_ge(ht_lo_done, u * (FT // FC) + (c + 1))
                    if c == 0:
                        if isinstance(u, int) and u == 0:
                            pe.wait_ge(y_copied, STEPS)
                        at_least(pe, z_scaled, u * NT)
                    for t in range(NT):
                        parts = [(f, part[i]) for f in range(c * FC, (c + 1) * FC) for part in (ht_hi, ht_lo)]
                        for n, (f, part) in enumerate(parts):
                            last = nc.tensor.matmul(Y_BANK[:, t * E:(t + 1) * E], part[:, f, t * P:(t + 1) * P],
                                                    wpr_t[:, f, :], start=c == 0 and t == 0 and n == 0, stop=f == FT - 1,
                                                    skip_group_check=True)
                last.then_inc(z_ready, 1)

            def step(u0, s):
                at = unit_at(u0, s, FLAG["up"])
                if at:
                    up(*at, 0)
                at = unit_at(u0, s, FLAG["up"])
                if at:
                    up(*at, 1)
                at = unit_at(u0, s, FLAG["down"])
                if at:
                    u, i = at
                    down(u, i)
                at = unit_at(u0, s, FLAG["up"])
                if at:
                    up(*at, 2)
                at = unit_at(u0, s, FLAG["turn"])
                if at:
                    u, i = at
                    pe.wait_ge(x2_norm, u * NT + NT)
                    if isinstance(u, int) and u == 0:
                        pe.wait_ge(wt_copied, CHUNKS)
                    at_least(pe, x2_lo_done, u)
                    for k in range(ET):
                        for t in range(NT):
                            last = nc.tensor.transpose(F_BANK[:, k * N + t * P:k * N + (t + 1) * P],
                                                       x2n[i][:, t, k * P:(k + 1) * P], ident[:, :])
                    last.then_inc(x2_turned, 1)
                at = unit_at(u0, s, FLAG["down"])
                if at:
                    u, i = at
                    pe.wait_ge(h_summed, u + 1)
                    at_least(pe, rms_eps, u)
                    for t in range(NT):
                        last = nc.tensor.matmul(O_BANK[:, t:t + 1], sums[i][:, t * P:(t + 1) * P], ones[:, :], start=t == 0,
                                                stop=True, skip_group_check=True)
                    last.then_inc(sum_ready, 1)
                at = unit_at(u0, s, FLAG["up"])
                if at:
                    up(*at, 3)

            def batch(g0, par, steps):
                for s in range(steps):
                    turn(g0, par, s)
                    score(g0, par, s)
                    value(g0, par, s)
                    c0 = front_at(g0, s, "keys")
                    if c0 is not None:
                        project_keys(c0, 1 - par)
                    weights_turn(g0, s)
                    c0 = front_at(g0, s, "turn")
                    if c0 is not None:
                        turn_x(c0, 1 - par)
                    c0 = front_at(g0, s, "values")
                    if c0 is not None:
                        project_values(c0, 1 - par)
                    for i in later_turns(g0, s):
                        turn_weight(i)
                    project(g0, par, s)
                    if isinstance(g0, int) and g0 + s == 0:
                        project_values(0, 0)
                    if isinstance(g0, int) and g0 + s == 1:
                        turn_vh(0, 0)
                    project_out(g0, par, s)
                    c0 = front_at(g0, s, "turn_vh")
                    if c0 is not None:
                        turn_vh(c0, 1 - par)
                    early_unit_step(g0, s, step)

            pe.wait_ge(consts, 2)
            turn_weight(0)
            turn_weight(1)
            turn_x(0, 0)
            for i in range(2, LATER):
                turn_weight(i)
            project_keys(0, 0)
            over_batches(pe, batch)
            over_units(pe, step)

        @block.scalar
        def _(act):
            def weight_hi(i):
                what, hi, _, b, _ = turns[i]
                o, view = turn_target(what, hi)
                act.wait_ge(w_turned, i + 1)
                nc.scalar.activation(o, view(bank[b]), ACT.Copy).then_inc(w_hi_done, 1)

            def split_x(c0, par):
                act.wait_ge(xt_turned, c0 + PAIRS)
                at_least(act, q_ready, c0 - PAIRS)
                nc.scalar.activation(xt_hi[par][:, :, :].rearrange("p k n -> p (k n)"), F_BANK, ACT.Copy)\
                    .then_inc(xt_hi_done, PAIRS)

            def keys_and_gates(c0, par):
                act.wait_ge(kg_ready, c0 + PAIRS)
                at_least(act, k_ready, c0)
                nc.scalar.activation(k_swap[0:D // 2, :], F_BANK[D // 2:D, 0:N], ACT.Copy).then_inc(k_swapped, PAIRS // 2)
                nc.scalar.activation(k_swap[D // 2:D, :], F_BANK[0:D // 2, 0:N], ACT.Copy).then_inc(k_swapped, PAIRS // 2)
                at_least(act, decay_done, c0)
                nc.scalar.activation(gate_e[0:2 * H, :], F_BANK[2 * H:4 * H, N:2 * N], ACT.Exp, scale=-1.0)\
                    .then_inc(gate_exp, PAIRS)

            def values_hi(c0, par):
                act.wait_ge(v_ready, c0 + PAIRS)
                at_least(act, o_ready, c0 - PAIRS)
                nc.scalar.activation(vals_hi[par][:, :, :].rearrange("p t d -> p (t d)"), F_BANK[:, 0:N], ACT.Copy)\
                    .then_inc(v_hi_done, PAIRS)

            def copy_y(c0):
                act.wait_ge(y_added, c0 + PAIRS)
                act.wait_ge(ln2_done, c0 + PAIRS)
                nc.scalar.activation(y_sb.rearrange("p t e -> p (t e)"), Y_BANK, ACT.Copy).then_inc(y_copied, PAIRS)

            def swap(g0, s):
                at = pair_at(g0, s, LAG["rope"])
                if at:
                    g, p, _ = at
                    half = D // 2
                    act.wait_ge(q_ready, g + 1)
                    at_least(act, q_roped, g - 1)
                    flat = q_swap[p % 2].rearrange("p h n -> p (h n)")
                    nc.scalar.activation(flat[0:half, :], Q_BANK[half:D, :], ACT.Copy)
                    nc.scalar.activation(flat[half:D, :], Q_BANK[0:half, :], ACT.Copy).then_inc(q_swapped, 1)

            def exponent(g0, s):
                at = pair_at(g0, s, LAG["softmax"])
                if at:
                    g, p, _ = at
                    tb = T[p % 4]
                    late = tb[:, 0:4 * P].rearrange("p (t h m) -> p t h m", t=NT, h=HP)
                    act.wait_ge(s_max, g + 1)
                    at_least(act, p_inv, g - 3)
                    for j in range(HP):
                        nc.scalar.activation(late[:, :, j, :], late[:, :, j, :], ACT.Exp, bias=nmax[p % 4][:, j:j + 1],
                                             accum_out=rsum[p % 4][:, j:j + 1])
                    for j in range(HP):
                        early = tb[:, (4 + j) * P:(5 + j) * P]
                        last = nc.scalar.activation(early, early, ACT.Exp, bias=nmax[p % 4][:, 2 + j:3 + j],
                                                    accum_out=rsum[p % 4][:, 2 + j:3 + j])
                    last.then_inc(p_exp, 1)

            def normalise(g0, s):
                at = pair_at(g0, s, LAG["softmax"])
                if at and in_last_batch(at[0]):
                    g, p, _ = at
                    tb, r = T[p % 4], rinv[p % 4]
                    late = tb[:, 0:4 * P].rearrange("p (t h m) -> p t h m", t=NT, h=HP)
                    act.wait_ge(p_inv, g + 1)
                    for j in range(HP):
                        nc.scalar.activation(late[:, :, j, :], late[:, :, j, :], ACT.Copy, scale=r[:, j:j + 1])
                    for j in range(HP):
                        early = tb[:, (4 + j) * P:(5 + j) * P]
                        last = nc.scalar.activation(early, early, ACT.Copy, scale=r[:, 2 + j:3 + j])
                    last.then_inc(p_ready, 1)

            def weigh_pt(g0, par, s):
                at = pair_at(g0, s, LAG["turn"])
                if at:
                    g, p, back = at
                    vh = vh_col[par ^ back]
                    act.wait_ge(pt_ready, g + 1)
                    at_least(act, pt_lo_done, g - 1)
                    if p == 0:
                        act.wait_ge(vh_copied, (g0 - PAIRS if back else g0) + PAIRS)
                    for t, (b, at_word, n) in enumerate(((PT0_BANK, 0, N), (PT1_BANK, 4 * P, P))):
                        for j in range(HP):
                            h = H + p * HP + j
                            last = nc.scalar.activation(pt[p % 2][:, at_word + j * n:at_word + (j + 1) * n],
                                                        b[:, j * n:(j + 1) * n], ACT.Copy, scale=vh[:, t, h:h + 1])
                    last.then_inc(pt_weighted, 1)

            def split_pt(g0, s):
                at = pair_at(g0, s, LAG["turn"])
                if at:
                    g, p, _ = at
                    act.wait_ge(pt_weighted, g + 1)
                    at_least(act, o_ready, g - 1)
                    nc.scalar.activation(pt_hi[p % 2], pt[p % 2], ACT.Copy).then_inc(pt_hi_done, 1)

            def split_o(g0, s):
                at = pair_at(g0, s, LAG["value"])
                if at:
                    g, p, _ = at
                    act.wait_ge(o_ready, g + 1)
                    at_least(act, y_added, g - 1)
                    nc.scalar.activation(o_hi[p % 2].rearrange("p h n -> p (h n)"), O_BANK, ACT.Copy).then_inc(o_hi_done, 1)

            def weights_cast(g0, s):
                c = chunk_at(g0, s, "cast")
                if c is not None:
                    act.wait_ge(wt_in[c % 2], c // 2 * 16 + 16)
                    act.wait_ge(k_ready, STEPS)
                    act.wait_ge(coef_done, STEPS)
                    at_least(act, wt_done, c - 2)
                    nc.scalar.activation(w_bf[c % 3], w_stage[c % 2], ACT.Copy).then_inc(wt_cast, 1)

            def weights_copy(g0, s):
                c = chunk_at(g0, s, "turn")
                if c is not None:
                    b = F_BANK.bitcast(BF16)
                    if c < CHUNKS - ET:
                        o = wgu_t[:, :, c * 512:(c + 1) * 512].rearrange("p k (t c) -> p t k c", c=P)
                        v = b.rearrange("p (t k c) -> p t k c", k=ET, c=P)
                    else:
                        j = c - (CHUNKS - ET)
                        o, v = wpr_t[:, :, j * P:(j + 1) * P], b.rearrange("p (f c) -> p f c", c=P)
                    act.wait_ge(wt_turned, c + 1)
                    nc.scalar.activation(o, v, ACT.Copy).then_inc(wt_copied, 1)

            def activate(u, i, c):
                act.wait_ge(gate_ready, u * (FT // FC) + (c + 1))
                at_least(act, h_ready, u * (FT // FC) + (c - 1))
                nc.scalar.activation(sig[c % 2], bank[c % 2 * 2], ACT.Silu).then_inc(gate_silu, 1)

            def high_hidden(u, i, c):
                tiles = slice(c * FC, (c + 1) * FC)
                act.wait_ge(h_ready, u * (FT // FC) + (c + 1))
                at_least(act, z_ready, u - 1)
                nc.scalar.activation(ht_hi[i][:, tiles, :], hid[i][:, tiles, :], ACT.Copy).then_inc(ht_hi_done, 1)

            def square_hidden(u, i, c):
                tiles = slice(c * FC, (c + 1) * FC)
                act.wait_ge(h_ready, u * (FT // FC) + (c + 1))
                at_least(act, h_summed, u - 1)
                nc.scalar.activation(squares[i][:, tiles, :], hid[i][:, tiles, :], ACT.Square).then_inc(h_squared, 1)

            def step(u0, s):
                at = unit_at(u0, s, FLAG["up"])
                if at:
                    activate(*at, 0)
                at = unit_at(u0, s, FLAG["up"])
                if at:
                    high_hidden(*at, 0)
                at = unit_at(u0, s, FLAG["up"])
                if at:
                    activate(*at, 1)
                at = unit_at(u0, s, FLAG["up"])
                if at:
                    high_hidden(*at, 1)
                at = unit_at(u0, s, FLAG["turn"])
                if at:
                    u, i = at
                    act.wait_ge(x2_turned, u + 1)
                    at_least(act, up_ready, (u - 1) * (FT // FC))
                    nc.scalar.activation(x2_hi[i][:, :, :].rearrange("p k n -> p (k n)"), F_BANK, ACT.Copy)\
                        .then_inc(x2_hi_done, 1)
                at = unit_at(u0, s, FLAG["up"])
                if at:
                    activate(*at, 2)
                at = unit_at(u0, s, FLAG["up"])
                if at:
                    square_hidden(*at, 1)
                at = unit_at(u0, s, FLAG["up"])
                if at:
                    activate(*at, 3)
                at = unit_at(u0, s, FLAG["up"])
                if at:
                    high_hidden(*at, 2)
                at = unit_at(u0, s, FLAG["up"])
                if at:
                    square_hidden(*at, 2)
                at = unit_at(u0, s, FLAG["up"])
                if at:
                    square_hidden(*at, 0)
                at = unit_at(u0, s, FLAG["up"])
                if at:
                    high_hidden(*at, 3)
                at = unit_at(u0, s, FLAG["up"])
                if at:
                    square_hidden(*at, 3)

            def batch(g0, par, steps):
                for s in range(steps):
                    swap(g0, s)
                    exponent(g0, s)
                    weigh_pt(g0, par, s)
                    split_o(g0, s)
                    c0 = front_at(g0, s, "turn")
                    if c0 is not None:
                        split_x(c0, 1 - par)
                    split_pt(g0, s)
                    c0 = front_at(g0, s, "keys")
                    if c0 is not None:
                        keys_and_gates(c0, 1 - par)
                    c0 = front_at(g0, s, "values")
                    if c0 is not None:
                        values_hi(c0, 1 - par)
                    normalise(g0, s)
                    c0 = tail_at(g0, s, "copy")
                    if c0 is not None:
                        copy_y(c0)
                    weights_cast(g0, s)
                    early_unit_step(g0, s, step)
                    for i in later_turns(g0, s):
                        weight_hi(i)
                    if isinstance(g0, int) and g0 + s == 0:
                        values_hi(0, 0)
                    weights_copy(g0, s)

            weight_hi(0)
            weight_hi(1)
            split_x(0, 0)
            for i in range(2, LATER):
                weight_hi(i)
            keys_and_gates(0, 0)
            over_batches(act, batch)
            over_units(act, step)

        @block.vector
        def _(dve):
            nc.vector.memset(whg_hi[:, :, 4 * H:P].bitcast(F32), 0.0).then_inc(ln2_done, PAIRS)
            nc.vector.memset(whg_lo[:, :, 4 * H:P].bitcast(F32), 0.0).then_inc(x1_done, PAIRS)
            nc.vector.memset(ones[:, :], 1.0)

            def weight_lo(i):
                what, hi, lo, b, _ = turns[i]
                o, view = turn_target(what, lo)
                dve.wait_ge(w_hi_done, i + 1)
                nc.vector.tensor_tensor(o, view(bank[b]), turn_target(what, hi)[0].bitcast(F32), ALU.subtract)\
                    .then_inc(w_lo_done, 1)

            def stats_x(c0):
                xs = x_tiles(c0)
                for t in range(NT):
                    nc.vector.bn_stats(ln1_stat[:, t, :], xs[:, t, :]).then_inc(ln1_stats, PAIRS // NT)

            def gather_x(c0):
                dve.wait_ge(ln1_stats, c0 + PAIRS)
                for t in range(NT):
                    nc.vector.bn_aggr(ln1_agg[:, t, :], ln1_stat[:, t, :]).then_inc(ln1_aggr, PAIRS // NT)

            def norm_x(c0, par):
                xs = x_tiles(c0)
                dve.wait_ge(ln1_inv, c0 + PAIRS)
                at_least(dve, xt_turned, c0)
                for t in range(NT):
                    nc.vector.tensor_scalar(xn[:, t, :], xs[:, t, :], ln1_agg[:, t, 0:1], ln1_rstd[:, t:t + 1],
                                            ALU.subtract, ALU.mult).then_inc(ln1_done, PAIRS // NT)

            def split_x(c0, par):
                dve.wait_ge(xt_hi_done, c0 + PAIRS)
                nc.vector.tensor_tensor(xt_lo[par][:, :, :].rearrange("p k n -> p (k n)"), F_BANK,
                                        xt_hi[par][:, :, :].rearrange("p k n -> p (k n)").bitcast(F32), ALU.subtract)\
                    .then_inc(xt_lo_done, PAIRS)

            rows = slice(0, 2 * H)

            def keys_cos(c0):
                dve.wait_ge(gate_exp, c0 + PAIRS)
                at_least(dve, k_ready, c0)
                nc.vector.tensor_tensor(k_cos, F_BANK[:, 0:N], cosk, ALU.mult).then_inc(k_cos_done, PAIRS)
                nc.vector.tensor_scalar(gate_e[rows, :], gate_e[rows, :], 1.0, None, ALU.add).then_inc(gate_one, PAIRS)

            def decays(c0):
                dve.wait_ge(gate_one, c0 + PAIRS)
                nc.vector.memset(decay[rows, 0:1], 1.0).then_inc(decay_done, PAIRS // 2)
                nc.vector.reciprocal(decay[rows, 1:N], gate_e[rows, 0:N - 1]).then_inc(decay_done, PAIRS // 2)

            def coefs(c0):
                dve.wait_ge(decay_done, c0 + PAIRS)
                nc.vector.tensor_tensor_scan(coef[rows, :], decay[rows, :], ones[rows, :].to_broadcast([2 * H, N]), 1.0,
                                             ALU.mult, ALU.mult)\
                    .then_inc(coef_done, PAIRS)

            def weigh_kv(c0):
                dve.wait_ge(coef_done, c0 + PAIRS)
                nc.vector.tensor_tensor(kvw[rows, :], F_BANK[rows, N:2 * N], coef[rows, :], ALU.mult)\
                    .then_inc(kvw_done, PAIRS)

            def sum_kv(c0, par):
                dve.wait_ge(kvw_done, c0 + PAIRS)
                at_least(dve, kh_stored, c0 * (16 // PAIRS) - 16)
                nc.vector.tensor_tensor_scan(kv_cum[par][rows, :], ones[rows, :].to_broadcast([2 * H, N]), kvw[rows, :], 0.0,
                                             ALU.mult, ALU.add)\
                    .then_inc(cum_done, PAIRS)

            def values_lo(c0, par):
                dve.wait_ge(v_hi_done, c0 + PAIRS)
                nc.vector.tensor_tensor(vals_lo[par][:, :, :].rearrange("p t d -> p (t d)"), F_BANK[:, 0:N],
                                        vals_hi[par][:, :, :].rearrange("p t d -> p (t d)").bitcast(F32), ALU.subtract)\
                    .then_inc(v_lo_done, PAIRS)

            def copy_vh(c0, par):
                dve.wait_ge(vh_turned, c0 + PAIRS)
                at_least(dve, pt_weighted, c0 - PAIRS)
                nc.vector.tensor_copy(vh_col[par][:, :, :].rearrange("p t h -> p (t h)"), F_BANK[:, 0:NT * 2 * H])\
                    .then_inc(vh_copied, PAIRS)

            def stats_y(c0):
                dve.wait_ge(y_copied, c0 + PAIRS)
                for t in range(NT):
                    nc.vector.bn_stats(ln2_stat[:, t, :], y_sb[:, t, :]).then_inc(ln2_stats, PAIRS // NT)

            def gather_y(c0):
                dve.wait_ge(ln2_stats, c0 + PAIRS)
                for t in range(NT):
                    nc.vector.bn_aggr(ln2_agg[:, t, :], ln2_stat[:, t, :]).then_inc(ln2_aggr, PAIRS // NT)

            def norm_y(c0):
                dve.wait_ge(ln2_inv, c0 + PAIRS)
                dve.wait_ge(x1_done, c0 + PAIRS)
                for t in range(NT):
                    nc.vector.tensor_scalar(y_norm[:, t, :], y_sb[:, t, :], ln2_agg[:, t, 0:1], ln2_rstd[:, t:t + 1],
                                            ALU.subtract, ALU.mult).then_inc(ln2_done, PAIRS // NT)

            def queries_cos(g0, s):
                at = pair_at(g0, s, LAG["rope"])
                if at:
                    g, p, _ = at
                    dve.wait_ge(q_swapped, g + 1)
                    at_least(dve, q_roped, g - 1)
                    nc.vector.tensor_tensor(q_cos[p % 2], heads(Q_BANK, N), cosq.unsqueeze(1).to_broadcast([P, HP, N]),
                                            ALU.mult).then_inc(q_cosined, 1)

            def weigh_scores(g0, s):
                at = pair_at(g0, s, LAG["score"])
                if at:
                    g, p, back = at
                    kh = kh_all[p % 4]
                    dve.wait_ge(s_ready, g + 1)
                    dve.wait_ge(kh_in[p % 4], ((g0 - PAIRS if back else g0) + p // 4 * 4) * 4 + 16)
                    at_least(dve, pt_ready, g - 3)
                    nc.vector.tensor_tensor(T[p % 4][:, 0:4 * P].rearrange("p (t h m) -> p t h m", t=NT, h=HP),
                                            S1_BANK.rearrange("p (t h m) -> p t h m", t=NT, h=HP),
                                            kh.rearrange("p h (t m) -> p t h m", t=NT), ALU.mult)
                    nc.vector.tensor_tensor(heads(T[p % 4][:, 4 * P:6 * P], P), heads(S0_BANK[:, 0:2 * P], P),
                                            kh[:, :, 0:P], ALU.mult).then_inc(s_weighted, 1)

            def maxima(g0, s):
                at = pair_at(g0, s, LAG["score"])
                if at:
                    g, p, _ = at
                    tb = T[p % 4]
                    dve.wait_ge(s_masked, g * 2 + 2)
                    nc.vector.tensor_reduce(nmax[p % 4][:, 0:HP], tb[:, 0:4 * P].rearrange("p (t h m) -> p h t m", t=NT, h=HP),
                                            AX.XY, ALU.max, negate=True)
                    nc.vector.tensor_reduce(nmax[p % 4][:, HP:2 * HP], heads(tb[:, 4 * P:6 * P], P), AX.X, ALU.max,
                                            negate=True).then_inc(s_max, 1)

            def invert_sums(g0, s):
                at = pair_at(g0, s, LAG["softmax"])
                if at:
                    g, p, _ = at
                    dve.wait_ge(p_exp, g + 1)
                    nc.vector.reciprocal(rinv[p % 4], rsum[p % 4]).then_inc(p_inv, 1)

            def normalise(g0, s):
                at = pair_at(g0, s, LAG["softmax"])
                if at and not in_last_batch(at[0]):
                    g, p, _ = at
                    tb, r = T[p % 4], rinv[p % 4]
                    late = tb[:, 0:4 * P].rearrange("p (t h m) -> p t h m", t=NT, h=HP)
                    dve.wait_ge(p_inv, g + 1)
                    for j in range(HP):
                        nc.vector.tensor_scalar(late[:, :, j, :], late[:, :, j, :], r[:, j:j + 1], None, ALU.mult)
                    for j in range(HP):
                        early = tb[:, (4 + j) * P:(5 + j) * P]
                        last = nc.vector.tensor_scalar(early, early, r[:, 2 + j:3 + j], None, ALU.mult)
                    last.then_inc(p_ready, 1)

            def split_o(g0, s):
                at = pair_at(g0, s, LAG["value"])
                if at:
                    g, p, _ = at
                    dve.wait_ge(o_hi_done, g + 1)
                    nc.vector.tensor_tensor(o_lo[p % 2].rearrange("p h n -> p (h n)"), O_BANK,
                                            o_hi[p % 2].rearrange("p h n -> p (h n)").bitcast(F32), ALU.subtract)\
                        .then_inc(o_lo_done, 1)

            def weights_sum(g0, s):
                c = chunk_at(g0, s, "sum")
                if c is not None:
                    dve.wait_ge(wt_cast, c + 1)
                    nc.vector.tensor_reduce(w_sums, heads(w_bf[c % 3], GROUP), AX.X, ALU.add, apply_absolute_value=True)\
                        .then_inc(wt_summed, 1)
                    dve.wait_ge(wt_summed, c + 1)
                    at_least(dve, wt_signed, c - 1)
                    nc.vector.tensor_scalar(w_scale[c % 2], w_sums, 1.0 / GROUP, 1e-8, ALU.mult, ALU.max)\
                        .then_inc(wt_scaled, 1)
                    at_least(dve, wt_compared, c)
                    nc.vector.tensor_scalar(w_half, w_sums, 0.5 / GROUP, 0.5e-8, ALU.mult, ALU.max).then_inc(wt_scaled, 1)

            def weights_compare(g0, s):
                c = chunk_at(g0, s, "compare")
                if c is not None:
                    w, q = w_bf[c % 3], w_signs[c % 2]
                    half = w_half.unsqueeze(2).to_broadcast([P, FF // GROUP, GROUP])
                    dve.wait_ge(wt_scaled, 2 * c + 2)
                    dve.wait_ge(cum_done, STEPS)
                    at_least(dve, wt_done, c - 1)
                    nc.vector.tensor_tensor(heads(q, GROUP), heads(w, GROUP), half, ALU.is_gt)
                    at_least(dve, wt_decided, c)
                    nc.vector.scalar_tensor_tensor(heads(w_other, GROUP), heads(w, GROUP), -1.0, half, ALU.mult, ALU.is_gt)\
                        .then_inc(wt_compared, 1)

            def weights_decide(g0, s):
                c = chunk_at(g0, s, "decide")
                if c is not None:
                    q = w_signs[c % 2]
                    dve.wait_ge(wt_compared, c + 1)
                    nc.vector.tensor_tensor(q, q, w_other, ALU.subtract).then_inc(wt_decided, 1)

            def weights_change(g0, s):
                c = chunk_at(g0, s, "change")
                if c is not None:
                    q = w_signs[c % 2]
                    dve.wait_ge(wt_signed, c + 1)
                    nc.vector.tensor_tensor(q, q, w_bf[c % 3], ALU.subtract).then_inc(wt_changed, 1)

            def weights_finish(g0, s):
                c = chunk_at(g0, s, "finish")
                if c is not None:
                    dve.wait_ge(wt_changed, c + 1)
                    at_least(dve, wt_turned, c - 1)
                    nc.vector.tensor_tensor(w_tern[c % 2], w_bf[c % 3], w_signs[c % 2], ALU.add).then_inc(wt_done, 1)

            def multiply(u, i, c):
                tiles = slice(c * FC, (c + 1) * FC)
                dve.wait_ge(gate_silu, u * (FT // FC) + (c + 1))
                dve.wait_ge(up_ready, u * (FT // FC) + (c + 1))
                at_least(dve, ht_lo_done, (u - 1) * (FT // FC))
                at_least(dve, h_squared, (u - 1) * (FT // FC))
                nc.vector.tensor_tensor(hid[i][:, tiles, :].rearrange("p f n -> p (f n)"), sig[c % 2], bank[c % 2 * 2 + 1],
                                        ALU.mult).then_inc(h_ready, 1)

            def step(u0, s):
                at = unit_at(u0, s, FLAG["up"])
                if at:
                    multiply(*at, 0)
                at = unit_at(u0, s, FLAG["norm"])
                if at:
                    u, i = at
                    dve.wait_ge(x2_inv, u + 1)
                    at_least(dve, x2_turned, u - 1)
                    for t in range(NT):
                        nc.vector.tensor_scalar(x2n[i][:, t, :], x_batch(u)[:, t, :], x2_agg[:, t, 0:1], x2_rstd[:, t:t + 1],
                                                ALU.subtract, ALU.mult).then_inc(x2_norm, 1)
                at = unit_at(u0, s, FLAG["sum"])
                if at:
                    u, i = at
                    dve.wait_ge(h_squared, u * (FT // FC) + FT // FC)
                    at_least(dve, sum_ready, u - 1)
                    nc.vector.tensor_reduce(sums[i], squares[i].rearrange("p f n -> p n f"), AX.X, ALU.add)\
                        .then_inc(h_summed, 1)
                at = unit_at(u0, s, FLAG["stats"])
                if at:
                    u, i = at
                    dve.wait_ge(x1_done, u * PAIRS + 2 * PAIRS)
                    for t in range(NT):
                        nc.vector.bn_stats(x2_stat[:, t, :], x_batch(u)[:, t, :]).then_inc(x2_stats, 1)
                at = unit_at(u0, s, FLAG["up"])
                if at:
                    multiply(*at, 1)
                at = unit_at(u0, s, FLAG["stats"])
                if at:
                    u, i = at
                    dve.wait_ge(x2_stats, u * NT + NT)
                    for t in range(NT):
                        nc.vector.bn_aggr(x2_agg[:, t, :], x2_stat[:, t, :]).then_inc(x2_aggr, 2)
                at = unit_at(u0, s, FLAG["down"])
                if at:
                    u, i = at
                    dve.wait_ge(sum_ready, u + 1)
                    at_least(dve, z_scaled, (u - 1) * NT)
                    nc.vector.tensor_scalar(rms[i], O_BANK[:, 0:NT], FF * RMS_EPS, None, ALU.add).then_inc(rms_eps, 1)
                at = unit_at(u0, s, FLAG["turn"])
                if at:
                    u, i = at
                    dve.wait_ge(x2_hi_done, u + 1)
                    nc.vector.tensor_tensor(x2_lo[i][:, :, :].rearrange("p k n -> p (k n)"), F_BANK,
                                            x2_hi[i][:, :, :].rearrange("p k n -> p (k n)").bitcast(F32), ALU.subtract)\
                        .then_inc(x2_lo_done, 1)
                at = unit_at(u0, s, FLAG["up"])
                if at:
                    multiply(*at, 2)
                at = unit_at(u0, s, FLAG["z"])
                if at:
                    u, i = at
                    dve.wait_ge(rms_done, u + 1)
                    dve.wait_ge(z_ready, u + 1)
                    at_least(dve, z_norm, (u - 1) * NT)
                    for t in range(NT):
                        nc.vector.tensor_scalar(z[i][:, t, :], Y_BANK[:, t * E:(t + 1) * E], rms[i][:, t:t + 1],
                                                float(np.sqrt(FF)), ALU.mult, ALU.mult).then_inc(z_scaled, 1)
                at = unit_at(u0, s, FLAG["z"])
                if at:
                    u, i = at
                    dve.wait_ge(z_scaled, u * NT + NT)
                    for t in range(NT):
                        nc.vector.bn_stats(z_stat[:, t, :], z[i][:, t, :]).then_inc(z_stats, 1)
                at = unit_at(u0, s, FLAG["up"])
                if at:
                    u, i = at
                    multiply(u, i, 3)
                at = unit_at(u0, s, FLAG["z"])
                if at:
                    u, i = at
                    dve.wait_ge(z_stats, u * NT + NT)
                    for t in range(NT):
                        nc.vector.bn_aggr(z_agg[:, t, :], z_stat[:, t, :]).then_inc(z_aggr, 2)
                at = unit_at(u0, s, FLAG["z"])
                if at:
                    u, i = at
                    dve.wait_ge(z_inv, u + 1)
                    at_least(dve, res_done, u - 1)
                    for t in range(NT):
                        nc.vector.tensor_scalar(zn[i][:, t, :], z[i][:, t, :], z_agg[:, t, 0:1], z_rstd[:, t:t + 1],
                                                ALU.subtract, ALU.mult).then_inc(z_norm, 1)

            def batch(g0, par, steps):
                if isinstance(g0, int) and g0 == 0:
                    dve.wait_ge(x_second, 16)
                for s in range(steps):
                    c0 = front_at(g0, s, "stats")
                    if c0 is not None:
                        stats_x(c0)
                    queries_cos(g0, s)
                    c0 = front_at(g0, s, "norm")
                    if c0 is not None:
                        norm_x(c0, 1 - par)
                    c0 = front_at(g0, s, "decay")
                    if c0 is not None:
                        decays(c0)
                    weigh_scores(g0, s)
                    c0 = tail_at(g0, s, "stats")
                    if c0 is not None:
                        stats_y(c0)
                    invert_sums(g0, s)
                    c0 = tail_at(g0, s, "invert")
                    if c0 is not None:
                        gather_y(c0)
                    c0 = front_at(g0, s, "stats")
                    if c0 is not None:
                        gather_x(c0)
                    c0 = tail_at(g0, s, "norm")
                    if c0 is not None:
                        norm_y(c0)
                    normalise(g0, s)
                    maxima(g0, s)
                    c0 = front_at(g0, s, "coef")
                    if c0 is not None:
                        coefs(c0)
                    split_o(g0, s)
                    c0 = front_at(g0, s, "weigh")
                    if c0 is not None:
                        weigh_kv(c0)
                    c0 = front_at(g0, s, "sums")
                    if c0 is not None:
                        sum_kv(c0, 1 - par)
                    c0 = front_at(g0, s, "turn")
                    if c0 is not None:
                        split_x(c0, 1 - par)
                    c0 = front_at(g0, s, "gates")
                    if c0 is not None:
                        keys_cos(c0)
                    c0 = front_at(g0, s, "copy_vh")
                    if c0 is not None:
                        copy_vh(c0, 1 - par)
                    for i in later_turns(g0, s):
                        weight_lo(i)
                    if isinstance(g0, int) and g0 + s == 0:
                        values_lo(0, 0)
                    if isinstance(g0, int) and g0 + s == 1:
                        copy_vh(0, 0)
                    weights_change(g0, s)
                    weights_finish(g0, s)
                    weights_sum(g0, s)
                    weights_compare(g0, s)
                    weights_decide(g0, s)
                    early_unit_step(g0, s, step)
                    c0 = front_at(g0, s, "values")
                    if c0 is not None:
                        values_lo(c0, 1 - par)
                if isinstance(g0, int) and g0 == 0:
                    dve.wait_ge(x_half, 16)
                    dve.wait_ge(x_rest, 16)

            dve.wait_ge(x_first, 16)
            stats_x(0)
            gather_x(0)
            weight_lo(0)
            weight_lo(1)
            norm_x(0, 0)
            split_x(0, 0)
            for i in range(2, LATER):
                weight_lo(i)
            dve.wait_ge(tables_in, 16)
            keys_cos(0)
            decays(0)
            coefs(0)
            weigh_kv(0)
            sum_kv(0, 0)
            over_batches(dve, batch)
            over_units(dve, step)


def rope_tables():
    d = np.arange(0, D, 2, dtype=np.float32)
    inv = (ROPE_BASE ** (-d.astype(np.float64) / D)).astype(np.float32)
    ang = (np.arange(N, dtype=np.float32)[None, :] * inv[:, None]).astype(np.float64)
    cos, sin = np.cos(ang), np.sin(ang)
    c, s = np.concatenate([cos, cos]), np.concatenate([-sin, sin])
    return np.stack([c, s, c / np.sqrt(D), s / np.sqrt(D)], axis=1).astype(np.float32)


_INS = ["L0_attn_x", "L0_attn_Wq", "L0_attn_Wkv", "L0_attn_Wkvh", "L0_attn_Wg", "L0_attn_Wout", "L0_ffn_w_gate_up",
        "L0_ffn_w_proj"]


def kernel(**inputs):
    import concourse.bacc as bacc
    from concourse.bass_utils import run_bass_kernel_spmd

    nc = bacc.Bacc("TRN2", target_bir_lowering=False, num_devices=1)
    arrays = {name: np.ascontiguousarray(inputs[name]) for name in _INS}
    arrays["rope_tables"] = rope_tables()
    args = [nc.dram_tensor(name, a.shape, F32, kind="ExternalInput").ap() for name, a in arrays.items()]
    out = nc.dram_tensor("out", (BATCH, N, E), F32, kind="ExternalOutput").ap()
    sandwich_kernel(nc, *args, out)
    return run_bass_kernel_spmd(nc, [arrays], core_ids=[0]).results[0]["out"]
```
